# Optimizing a Trainium2 kernel written in Bass

```python
import numpy as np
import jax
import jax.numpy as jnp

def _softmax(x, axis=-1):
    return jax.nn.softmax(x, axis=axis)

def _gelu(x):
    return jax.nn.gelu(x, approximate=True)

def _silu(x):
    return jax.nn.silu(x)

def _sigmoid(x):
    return jax.nn.sigmoid(x)

def _layernorm(x, axis=-1, eps=1e-05):
    m = jnp.mean(x, axis=axis, keepdims=True)
    v = jnp.var(x, axis=axis, keepdims=True)
    return (x - m) / jnp.sqrt(v + eps)

def _scatter_add(tgt, idx, src, axis=0):
    return tgt.at[idx].add(src)

def _segment_sum(src, seg, n):
    return jax.ops.segment_sum(src, seg, n)
kernel_name = 'mk_gnn_resnorm_d1_gnn_r8_658456'

def setup_inputs(seed: int=0):
    np.random.seed(seed)
    _w = jnp.asarray

    def _rec_inputs():
        import jax
        import jax.numpy as jnp
        _gk = jax.random.key(seed)
        x = -0.0005121 + 1.001 * jax.random.normal(jax.random.fold_in(_gk, 1), (12500, 64), jnp.float32)
        src = jax.random.randint(jax.random.fold_in(_gk, 2), (400000,), 0, 12500, jnp.int32)
        dst = jnp.minimum((12500 * jax.random.uniform(jax.random.fold_in(_gk, 3), (400000,)) ** 2.0).astype(jnp.int32), 99999)
        _o = jnp.argsort(dst, stable=True)
        src = src[_o]
        dst = dst[_o]
        edge_attr_64 = -9.77346e-05 + 0.999888 * jax.random.normal(jax.random.fold_in(_gk, 12), (400000, 64), jnp.float32)
        return (x, src, dst, edge_attr_64)
    x, src, dst, edge_attr_64 = _rec_inputs()

    def _L0_gnn_setup():
        import jax, jax.numpy as jnp
        import numpy as np
        N_NODES = 6250
        N_EDGES = 100000
        NDIM_IN = 64
        EDIM = 64
        NDIM_OUT = 64
        key = jax.random.key(seed)
        ks = jax.random.split(key, 8)

        def xav(k, shape):
            fan_in, fan_out = (shape[0], shape[-1])
            std = np.sqrt(2.0) * np.sqrt(2.0 / (fan_in + fan_out))
            return jax.random.normal(k, shape, dtype=jnp.float32) * std
        return {'nfeats': jax.random.normal(ks[0], (N_NODES, NDIM_IN), dtype=jnp.float32), 'efeats': jax.random.normal(ks[1], (N_EDGES, EDIM), dtype=jnp.float32), 'W_ne': xav(ks[2], (NDIM_IN + EDIM, NDIM_OUT)), 'W_attn': xav(ks[3], (2 * NDIM_IN + EDIM, 1)), 'b_attn': jnp.zeros((1,), dtype=jnp.float32), 'W_out': xav(ks[4], (NDIM_IN + NDIM_OUT, NDIM_OUT)), 'src': jax.random.randint(ks[5], (N_EDGES,), 0, N_NODES, dtype=jnp.int64 if jax.config.jax_enable_x64 else jnp.int32), 'dst': jax.random.randint(ks[6], (N_EDGES,), 0, N_NODES, dtype=jnp.int64 if jax.config.jax_enable_x64 else jnp.int32)}
    _L0_gnn_all = _L0_gnn_setup()
    _L0_gnn_in = {k: v for k, v in _L0_gnn_all.items() if k in ('W_ne', 'W_attn', 'b_attn', 'W_out')}
    del _L0_gnn_all
    return {'x': x, 'src': src, 'dst': dst, 'edge_attr_64': edge_attr_64, 'L0_gnn_W_ne': _L0_gnn_in['W_ne'], 'L0_gnn_W_attn': _L0_gnn_in['W_attn'], 'L0_gnn_b_attn': _L0_gnn_in['b_attn'], 'L0_gnn_W_out': _L0_gnn_in['W_out']}

def reference(x, src, dst, edge_attr_64, L0_gnn_W_ne, L0_gnn_W_attn, L0_gnn_b_attn, L0_gnn_W_out):
    import jax
    import jax.numpy as jnp

    def _L0_gnn_ref(nfeats, efeats, W_ne, W_attn, b_attn, W_out, src, dst):
        import jax, jax.numpy as jnp
        import numpy as np
        N_NODES = 6250
        N_EDGES = 100000
        NDIM_IN = 64
        EDIM = 64
        NDIM_OUT = 64
        N = nfeats.shape[0]
        h_src = nfeats[src]
        h_dst = nfeats[dst]
        z_att = jnp.concatenate([h_src, h_dst, efeats], axis=-1)
        e = jax.nn.leaky_relu(z_att @ W_attn + b_attn, negative_slope=0.01)[:, 0]
        m = jnp.concatenate([h_src, efeats], axis=-1) @ W_ne
        emax = jax.ops.segment_max(e, dst, num_segments=N)
        ex = jnp.exp(e - emax[dst])
        denom = jax.ops.segment_sum(ex, dst, num_segments=N)
        alpha = ex / denom[dst]
        z = jax.ops.segment_sum(alpha[:, None] * m, dst, num_segments=N)
        out = jax.nn.relu(jnp.concatenate([nfeats, z], axis=-1) @ W_out)
        return out
    x = _layernorm(x + _L0_gnn_ref(x, edge_attr_64, L0_gnn_W_ne, L0_gnn_W_attn, L0_gnn_b_attn, L0_gnn_W_out, src, dst), axis=-1)
    return x

_drawn_inputs = setup_inputs


def setup_inputs(seed=0):
    import zlib

    import numpy as np

    out = dict(_drawn_inputs(seed))
    spreads = {}
    factors = {}
    for name, (base, spread) in spreads.items():
        noise = np.random.default_rng([zlib.crc32(name.encode()), seed]).standard_normal(out[name].shape)
        drawn = base * np.exp(spread * noise) if base else spread * noise
        out[name] = jnp.asarray(drawn.astype(out[name].dtype))
    for name, factor in factors.items():
        out[name] = (out[name] * factor).astype(out[name].dtype)
    return out
```

```python
from contextlib import ExitStack

import concourse.bass as bass
from concourse import mybir

F32 = mybir.dt.float32
BF16 = mybir.dt.bfloat16
I32 = mybir.dt.int32
U32 = mybir.dt.uint32
ALU = mybir.AluOpType
ACT = mybir.ActivationFunctionType
AX = mybir.AxisListType.X

P = 128
J = 8
ST = P * J
RING = 6
F = 64
ROW = 1 + F
VW = ROW + F + 1
AW = 2 * F + 1
NPART = 5 * J
SLOPE = 0.01
EPS = 1e-5
FAR = 2.0 ** 48
UNSEEN = 1e24
KEEP = 1e30
TINY = 1e-30
CB = 14


def graph_attention(nc, x, src, dst, ef, w_ne, w_att, b_att, w_out, out):
    N, E = x.shape[0], src.shape[0]
    NB = -(-N // P)
    NL = N - (NB - 1) * P
    NT = -(-E // ST)
    PL = (E - (NT - 1) * ST) // J
    TURNS = (NT - 1) // RING
    TC = -(-NT // P)
    OCT = NB // 8
    NR = NB - 8 * OCT
    assert TURNS * RING == NT - 1 and PL * J + (NT - 1) * ST == E
    assert 0 < NR <= 4 and OCT >= 1 and E >= ST
    TABLE = 16 * (-(-NB // CB) + (NB % CB != 1))
    chunks = [(b, min(CB, NB - b)) for b in range(0, NB, CB)]

    ctx = ExitStack()
    with ctx:
        def sb(name, shape, dt=F32):
            return ctx.enter_context(nc.sbuf_tensor(name, shape, dt))

        def ps(name, shape, dt=F32):
            return ctx.enter_context(nc.psum_tensor(name, shape, dt))

        def sem(name):
            return ctx.enter_context(nc.semaphore(name))

        table = nc.dram_tensor("node_table", (N, ROW), F32, kind="Internal").ap()
        bounds_i = nc.dram_tensor("bounds_i", (TC * P, 2), I32, kind="Internal").ap()
        bounds_f = nc.dram_tensor("bounds_f", (TC * P, 2), F32, kind="Internal").ap()

        ident = sb("ident", [P, P])
        identb = sb("identb", [P, P], BF16)
        sel_u = sb("sel_u", [NPART, J, P], BF16)
        sel_d = sb("sel_d", [NPART, J, P], BF16)
        pcol_i = sb("pcol_i", [P, 1], I32)
        pcol = sb("pcol", [P, 1])
        wcol_i = sb("wcol_i", [P, NB + 1], I32)
        wshift = sb("wshift", [P, NB + 1])
        wa = sb("wa", [P, 3 * F])
        ba = sb("ba", [P, 1])
        wne = sb("wne", [P, F])
        wneT = sb("wneT", [F, P])
        wo_x = sb("wo_x", [F, F])
        wo_z = sb("wo_z", [F, F])
        wz = sb("wz", [P, F])
        xt = sb("xt", [P, NB, ROW])
        y0 = sb("y0", [P, NB, F])
        acc = sb("acc", [P, (NB + 1) * AW])
        accv = acc[:, :].rearrange("p (b f) -> p b f", f=AW)
        node = sb("node", [P, NB + 1, 2])
        V = sb("V", [P, RING, J, VW])
        srcs = sb("srcs", [P, RING, J], U32)
        dparts = sb("dparts", [P, NT, 2 * J], BF16)
        trip = sb("trip", [1, TC * P * 2], I32)
        lowf = sb("lowf", [P, NT, 2])
        nidbias = sb("nidbias", [P, NT])
        half = sb("half", [P, NT, 2])
        keep = sb("keep", [P, NT, 2])
        low = sb("low", [P, TC, 2])
        low_i = sb("low_i", [P, TC, 4], I32)
        bi = sb("bi", [P, TC, 2], I32)
        bf = sb("bf", [P, TC, 2])
        prod = sb("prod", [P, 1024])
        q = sb("q", [P, J])
        u = sb("u", [P, J])
        urest = sb("urest", [P, J])
        parts = sb("parts", [P, NPART], BF16)
        partsT = sb("partsT", [NPART, P], BF16)
        ubc = sb("ubc", [P, 2, ST])
        sqd = sb("sqd", [P, ST])
        um = sb("um", [P, ST])
        e1 = sb("e1", [P, ST])
        e2 = sb("e2", [P, ST])
        pT = sb("pT", [P, 2, 512])
        nbias = sb("nbias", [P, 1])
        wnode = sb("wnode", [P, 2])
        cmax = sb("cmax", [P, 1])
        nt = sb("nt", [P, 1])
        ne = sb("ne", [P, 1])
        nn = sb("nn", [P, 1])
        ebias = sb("ebias", [P, 2])
        dif = sb("dif", [P, 1])
        dif2 = sb("dif2", [P, 2])
        alpha = sb("alpha", [P, 2])
        rl = sb("rl", [P, NB])
        ssum = sb("ssum", [P, NB])
        mean = sb("mean", [P, 8])
        rstd = sb("rstd", [P, NB])

        raw = acc[:, :].bitcast(I32)
        dst_e = raw[:, 0:NT * J].rearrange("p (t j) -> p t j", j=J)
        dst_s = raw[:, NT * J:2 * NT * J].rearrange("p (t j) -> p t j", j=J)
        dst_t = raw[:, 2 * NT * J:2 * NT * J + TC * ST].rearrange("p (c e) -> p c e", c=TC)

        psU = ps("psU", [P, 512])
        psTP = psU[0:NPART, 0:P // 2].bitcast(BF16)
        psD = ps("psD", [P, 2, ST])
        psT = ps("psT", [P, 2, 512])
        psG = ps("psG", [P, 512])

        w_in = sem("w_in")
        x_in = [sem(f"x_in{c}") for c in range(len(chunks))]
        xr_in = sem("xr_in")
        dt_in = sem("dt_in")
        de_in = sem("de_in")
        idx_in = [sem(f"idx_in{s}") for s in range(RING)]
        ef_in = [sem(f"ef_in{s}") for s in range(RING)]
        h_in = [sem(f"h_in{s}") for s in range(RING)]
        table_out = sem("table_out")
        bounds_out = sem("bounds_out")
        trip_in = sem("trip_in")
        lowf_in = sem("lowf_in")
        out_done = sem("out_done")
        pool_step = sem("pool_step")
        consts = sem("consts")
        dve_step = sem("dve_step")
        xpad = sem("xpad")
        dpad = sem("dpad")
        as_ready = sem("as_ready")
        bounds_ready = sem("bounds_ready")
        wt_ready = sem("wt_ready")
        wt_copied = sem("wt_copied")
        wz_ready = sem("wz_ready")
        wz_copied = sem("wz_copied")
        xs_ready = sem("xs_ready")
        xs_turned = sem("xs_turned")
        xs_copied = sem("xs_copied")
        y_ready = sem("y_ready")
        y_copied = sem("y_copied")
        v_free = [sem(f"v_free{s}") for s in range(RING)]
        nbias_ready = sem("nbias_ready")
        sq_done = sem("sq_done")
        m_done = sem("m_done")
        e_done = sem("e_done")
        mx_done = sem("mx_done")
        dif_done = sem("dif_done")
        al_done = sem("al_done")
        parts_done = sem("parts_done")
        tp_done = sem("tp_done")
        tp_copied = sem("tp_copied")
        bcu0 = sem("bcu0")
        bcu1 = sem("bcu1")
        bcd = sem("bcd")
        u0_copied = sem("u0_copied")
        u1_copied = sem("u1_copied")
        tr = [sem("tr0"), sem("tr1")]
        pt = [sem("pt0"), sem("pt1")]
        agg_done = sem("agg_done")
        merged = sem("merged")
        node_set = sem("node_set")
        wn0 = sem("wn0")
        wn1 = sem("wn1")
        prod_done = sem("prod_done")
        q_done = sem("q_done")
        cmax_done = sem("cmax_done")
        nt_done = sem("nt_done")
        ne_done = sem("ne_done")
        nn_done = sem("nn_done")
        d_done = sem("d_done")
        scaled = sem("scaled")
        u_done = sem("u_done")
        p0_done = sem("p0_done")
        r_done = sem("r_done")
        p1_done = sem("p1_done")
        all_merged = sem("all_merged")
        z_ready = sem("z_ready")
        z_turned = sem("z_turned")
        z_copied = sem("z_copied")
        o_ready = sem("o_ready")
        o_read = sem("o_read")
        cen_done = sem("cen_done")
        sq_ready = sem("sq_ready")
        var_ready = sem("var_ready")
        std_ready = sem("std_ready")
        fin_step = sem("fin_step")
        rows_ready = sem("rows_ready")

        block = ctx.enter_context(nc.Block())

        def edge_rows(dram, t):
            return dram[bass.ds(t * ST, ST)] if not isinstance(t, int) else dram[t * ST:(t + 1) * ST]

        @block.sync
        def _(sp):
            sp.dma_start(wa[:, :], w_att.rearrange("a b -> b a").broadcast_to((P, 3 * F))).then_inc(w_in, 16)
            sp.dma_start(ba[:, :], b_att.rearrange("(a b) -> a b", a=1).broadcast_to((P, 1))).then_inc(w_in, 16)
            sp.dma_start(wne[:, :], w_ne[:, :]).then_inc(w_in, 16)
            sp.dma_start(wo_x[:, :], w_out[0:F, :]).then_inc(w_in, 16)
            sp.dma_start(wo_z[:, :], w_out[F:2 * F, :]).then_inc(w_in, 16)
            full = NT - 1
            for c in range(TC):
                n = min(P, full - c * P)
                if n > 0:
                    sp.dma_start(dst_t[0:n, c, :], dst[c * ST * P:c * ST * P + n * ST].rearrange("(p e) -> p e", e=ST)).then_inc(dt_in, 16)
            pl = full - (TC - 1) * P
            sp.dma_start(dst_t[pl:pl + 1, TC - 1, :], dst[E - ST:E].rearrange("(p e) -> p e", e=ST)).then_inc(dt_in, 16)
            sp.wait_ge(dpad, 1)
            sp.dma_start(dst_e[:, 0:full, :], dst[0:full * ST].rearrange("(t p j) -> p t j", p=P, j=J)).then_inc(de_in, 16)
            sp.dma_start(dst_e[0:PL, full, :], dst[full * ST:E].rearrange("(p j) -> p j", j=J)).then_inc(de_in, 16)

            def load(t, s):
                sp.dma_start(srcs[:, s, :], edge_rows(src, t).rearrange("(p j) -> p j", j=J).bitcast(U32)).then_inc(idx_in[s], 16)
                sp.dma_start(V[:, s, :, ROW:ROW + F], (ef[bass.ds(t * ST, ST), :]).rearrange("(p j) f -> p j f", j=J)).then_inc(ef_in[s], 16)

            for s in range(RING):
                load(s, s)
            sp.wait_ge(bounds_ready, 2)
            sp.dma_start(bounds_i.rearrange("(c p) k -> p c k", p=P), bi[:, :, :]).then_inc(bounds_out, 16)
            sp.dma_start(bounds_f.rearrange("(c p) k -> p c k", p=P), bf[:, :, :]).then_inc(bounds_out, 16)
            sp.wait_ge(bounds_out, 32)
            sp.dma_start(trip[:, :], bounds_i.rearrange("t k -> (t k)").rearrange("(a b) -> a b", a=1)).then_inc(trip_in, 16)
            sp.dma_start(lowf[:, :, :], bounds_f[0:NT, :].rearrange("t k -> (t k)").rearrange("(a b) -> a b", a=1).broadcast_to((P, NT * 2)).rearrange("p (t k) -> p t k", k=2)).then_inc(lowf_in, 16)
            with sp.Fori(1, TURNS) if TURNS > 1 else ExitStack() as k:
                if TURNS > 1:
                    for s in range(RING):
                        sp.wait_ge(v_free[s], k + (1 if s == RING - 1 else 0))
                        load(RING * k + s, s)
            sp.wait_ge(v_free[0], TURNS)
            sp.dma_start(srcs[0:PL, 0, :], src[full * ST:E].rearrange("(p j) -> p j", j=J).bitcast(U32)).then_inc(idx_in[0], 16)
            sp.dma_start(V[0:PL, 0, :, ROW:ROW + F], ef[full * ST:E, :].rearrange("(p j) f -> p j f", j=J)).then_inc(ef_in[0], 16)
            for o in range(OCT):
                sp.wait_ge(rows_ready, o + 1)
                sp.dma_start(out[o * 8 * P:(o + 1) * 8 * P, :].rearrange("(b p) f -> p b f", p=P), y0[:, 8 * o:8 * o + 8, :]).then_inc(out_done, 16)
            sp.wait_ge(rows_ready, OCT + 1)
            n = NR - 1
            outs = OCT + 1
            if n:
                sp.dma_start(out[8 * OCT * P:(NB - 1) * P, :].rearrange("(b p) f -> p b f", p=P), y0[:, 8 * OCT:NB - 1, :]).then_inc(out_done, 16)
                outs += 1
            sp.dma_start(out[(NB - 1) * P:N, :], y0[0:NL, NB - 1, :]).then_inc(out_done, 16)
            sp.wait_ge(out_done, 16 * outs)

        @block.gpsimd
        def _(pool):
            step = 0
            for ap in (ident[:, :], identb[:, :], sel_u[:, :, :], sel_d[:, :, :]):
                nc.gpsimd.memset(ap, 0.0).then_inc(pool_step, 1)
                step += 1
            pool.wait_ge(pool_step, step)
            for t_ in (ident, identb):
                nc.gpsimd.affine_select(out=t_[:, :], in_=t_[:, :], compare_op=ALU.not_equal, fill=1.0, base=0,
                                        pattern=[[-1, P]], channel_multiplier=1).then_inc(pool_step, 1)
                step += 1
            for t_, row, fill in ((sel_u, 0, 1.0), (sel_u, J, 1.0), (sel_u, 2 * J, 1.0),
                                  (sel_d, 3 * J, 1.0), (sel_d, 4 * J, float(P))):
                nc.gpsimd.affine_select(out=t_[:, :, :], in_=t_[:, :, :], compare_op=ALU.not_equal, fill=fill,
                                        base=-row, pattern=[[-1, J], [0, P]], channel_multiplier=1).then_inc(pool_step, 1)
                step += 1
                pool.wait_ge(pool_step, step)
            nc.gpsimd.iota(pcol_i[:, :], pattern=[[0, 1]], base=0, channel_multiplier=1).then_inc(consts, 1)
            nc.gpsimd.iota(wcol_i[:, :], pattern=[[1, NB + 1]], base=0, channel_multiplier=0).then_inc(consts, 1)

            def gather(s, n):
                for j in range(J):
                    nc.gpsimd.indirect_dma_start(V[0:n, s, j, 0:ROW], None, table[:, :],
                                                 bass.IndirectOffsetOnAxis(ap=srcs[0:n, s, j:j + 1], axis=0)).then_inc(h_in[s], 16)

            pool.wait_ge(table_out, TABLE)
            for s in range(RING):
                pool.wait_ge(idx_in[s], 16)
                gather(s, P)
            if TURNS > 1:
                arrived, freed_last = pool.alloc_register("arrived"), pool.alloc_register("freed_last")
                with pool.Fori(1, TURNS) as k:
                    pool.reg_mov(arrived, 16 * k + 16)
                    pool.reg_mov(freed_last, k + 1)
                    indices = pool.snap(arrived)
                    for s in range(RING):
                        freed = k if s < RING - 1 else pool.snap(freed_last)
                        pool.wait_ge(table_out, TABLE)
                        pool.wait_ge(idx_in[s], indices)
                        pool.wait_ge(v_free[s], freed)
                        gather(s, P)
            pool.wait_ge(idx_in[0], 16 * TURNS + 16)
            pool.wait_ge(v_free[0], TURNS)
            gather(0, PL)

            pool.wait_ge(all_merged, 1)

            def scale_group(b, n, par):
                nc.gpsimd.tensor_tensor(e1[:, par * 512:par * 512 + n * P].rearrange("p (b f) -> p b f", f=P),
                                        accv[:, b:b + n, 0:P] if isinstance(b, int) else accv[:, bass.ds(b, n), 0:P],
                                        (rl[:, b:b + n] if isinstance(b, int) else rl[:, bass.ds(b, n)]).unsqueeze(2).broadcast_to((P, n, P)),
                                        ALU.mult).then_inc(z_ready, 1)

            with pool.Fori(0, OCT) as o:
                for par in range(2):
                    pool.wait_ge(z_turned, 2 * o + par + 1)
                    scale_group(8 * o + 4 * par, 4, par)
            pool.wait_ge(z_turned, 2 * OCT + 1)
            scale_group(8 * OCT, NR, 0)

        @block.scalar
        def _(act):
            for c, (b, n) in enumerate(chunks):
                last = b + n == NB
                m = n - 1 if last else n
                if last:
                    act.wait_ge(xpad, 1)
                if m:
                    act.dma_start(xt[:, b:b + m, 1:ROW], x[b * P:(b + m) * P, :].rearrange("(b p) f -> p b f", p=P)).then_inc(x_in[c], 16)
                if last:
                    act.dma_start(xt[0:NL, NB - 1, 1:ROW], x[(NB - 1) * P:N, :]).then_inc(xr_in, 16)
            act.sem_inc(xs_copied, 2)
            act.sem_inc(y_copied, 2)
            for c, (b, n) in enumerate(chunks):
                last = b + n == NB
                m = n - 1 if last else n
                act.wait_ge(as_ready, c + 1)
                if m:
                    act.dma_start(table[b * P:(b + m) * P, :].rearrange("(b p) f -> p b f", p=P), xt[:, b:b + m, :]).then_inc(table_out, 16)
                if last:
                    act.dma_start(table[(NB - 1) * P:N, :], xt[0:NL, NB - 1, :]).then_inc(table_out, 16)
            act.wait_ge(wt_ready, 1)
            nc.scalar.copy(wneT[:, :], psG[0:F, 0:P]).then_inc(wt_copied, 1)
            act.wait_ge(wz_ready, 1)
            nc.scalar.copy(wz[:, :], psG[:, P:P + F]).then_inc(wz_copied, 1)

            def y_turn(n0, g, cnt, b):
                for par in range(cnt):
                    w = g if cnt == 1 else 4
                    act.wait_ge(xs_turned, n0 + par + 1)
                    nc.scalar.copy(e1[0:F, par * 512:par * 512 + w * P], psT[0:F, par, 0:w * P]).then_inc(xs_copied, 1)
                for par in range(cnt):
                    w = g if cnt == 1 else 4
                    act.wait_ge(y_ready, n0 + par + 1)
                    dst_ap = y0[:, b + 4 * par:b + 4 * par + w, :] if isinstance(b, int) else y0[:, bass.ds(b + 4 * par, w), :]
                    nc.scalar.copy(dst_ap, psD[:, par, 0:w * F].rearrange("p (b f) -> p b f", f=F)).then_inc(y_copied, 1)

            with act.Fori(0, OCT) as o:
                y_turn(2 * o, 4, 2, 8 * o)
            y_turn(2 * OCT, NR, 1, 8 * OCT)

            def stage_b_out(H, d, G=None):
                act.wait_ge(tp_done, H)
                nc.scalar.copy(partsT[:, :], psTP).then_inc(tp_copied, 1)
                act.wait_ge(bcu0, H)
                nc.scalar.copy(ubc[:, d, 0:512], psU[:, :]).then_inc(u0_copied, 1)
                if G is not None:
                    factors(G)
                act.wait_ge(bcu1, H)
                nc.scalar.copy(ubc[:, d, 512:ST], psU[:, :]).then_inc(u1_copied, 1)

            g = act.alloc_register("g_act")
            h = act.alloc_register("h_act")
            coming = act.alloc_register("coming_act")
            count = act.alloc_register("count_act")
            act.reg_mov(g, 1)
            act.reg_mov(h, 2)
            stage_b_out(1, 0)

            def weights_out(G):
                for i in range(2):
                    act.wait_ge(tr[i], G)
                    nc.scalar.copy(pT[:, i, :], psT[:, i, :]).then_inc(pt[i], 1)

            def factors(G):
                act.wait_ge(dif_done, G)
                nc.scalar.activation(alpha[:, :], dif2[:, :], ACT.Exp).then_inc(al_done, 1)

            def supertile(t, s, ahead):
                act.reg_mov(count, act.snap(coming))
                windows = act.snap(count, min_val=1, max_val=NB)
                d = s % 2
                if not ahead:
                    act.wait_ge(bcd, act.snap(g))
                with act.Fori(0, windows):
                    G, H = act.snap(g), act.snap(h)
                    if ahead:
                        act.wait_ge(bcd, G)
                    act.wait_ge(nbias_ready, G)
                    nc.scalar.activation(sqd[:, :], psD[:, d, :], ACT.Square, bias=nbias[:, 0:1], scale=FAR).then_inc(sq_done, 1)
                    weights_out(G)
                    act.wait_ge(m_done, G)
                    nc.scalar.activation(e1[:, :], um[:, :], ACT.Exp, bias=ebias[:, 0:1])
                    nc.scalar.activation(e2[:, :], um[:, :], ACT.Exp, bias=ebias[:, 1:2], scale=SLOPE).then_inc(e_done, 1)
                    if ahead:
                        act.load(coming, trip[0:1, bass.ds(2 * t + 3, 1)])
                        stage_b_out(H, 1 - d, G)
                    else:
                        factors(G)
                    act.reg_add(g, g, 1)
                    act.reg_add(h, h, 1)

            act.wait_ge(trip_in, 16)
            act.load(coming, trip[0:1, 1:2])
            with act.Fori(0, TURNS) as k:
                for s in range(RING):
                    supertile(RING * k + s, s, True)
            supertile(NT - 1, 0, False)
            weights_out(act.snap(g))

            def z_turn(n, par, w):
                act.wait_ge(z_turned, n + 3)
                nc.scalar.copy(pT[:, par, 0:w * P], psT[:, par, 0:w * P]).then_inc(z_copied, 1)

            def squares(o, w):
                act.wait_ge(cen_done, o + 1)
                yo = y0[:, bass.ds(8 * o, w), :] if not isinstance(o, int) else y0[:, 8 * o:8 * o + w, :]
                nc.scalar.activation(sqd[:, 0:w * F].rearrange("p (b f) -> p b f", f=F), yo, ACT.Square).then_inc(sq_ready, 1)

            with act.Fori(0, OCT) as o:
                for par in range(2):
                    z_turn(2 * o + par, par, 4)
                squares(o, 8)
            z_turn(2 * OCT, 0, NR)
            squares(OCT, NR)
            act.wait_ge(var_ready, 1)
            nc.scalar.activation(rstd[:, :], ssum[:, :], ACT.Sqrt).then_inc(std_ready, 1)

        @block.vector
        def _(dve):
            steps = [0]

            def step(ins):
                steps[0] += 1
                ins.then_inc(dve_step, 1)
                dve.wait_ge(dve_step, steps[0])

            nc.vector.memset(xt[:, NB - 1, :], 0.0).then_inc(xpad, 1)
            nc.vector.memset(dst_e[:, NT - 1, :], -P).then_inc(dpad, 1)
            nc.vector.memset(V[:, :, :, VW - 1:VW], 1.0)
            nc.vector.memset(node[:, :, 1:2], UNSEEN)
            nc.vector.memset(node[:, NB:NB + 1, 0:1], 0.0)
            nc.vector.memset(alpha[:, :], 1.0).then_inc(al_done, 1)
            nc.vector.memset(dif2[:, :], 0.0)
            nc.vector.memset(low[:, :, :], 0.0)
            step(nc.vector.memset(q[:, :], 0.0))
            dve.wait_ge(w_in, 16 * 5)

            def dot(b, n, w, dest):
                step(nc.vector.tensor_tensor(prod[:, 0:n * F].rearrange("p (b f) -> p b f", f=F), xt[:, b:b + n, 1:ROW],
                                             wa[:, w * F:(w + 1) * F].unsqueeze(1).broadcast_to((P, n, F)), ALU.mult))
                return nc.vector.tensor_reduce(dest, prod[:, 0:n * F].rearrange("p (b f) -> p b f", f=F), AX, ALU.add)

            for c, (b, n) in enumerate(chunks):
                if n > 1 or b + n < NB:
                    dve.wait_ge(x_in[c], 16)
                if b + n == NB:
                    dve.wait_ge(xr_in, 16)
                dot(b, n, 0, xt[:, b:b + n, 0]).then_inc(as_ready, 1)
                dve.wait_ge(as_ready, c + 1)

            loads = sum(1 for c in range(TC) if min(P, NT - 1 - c * P) > 0) + 1
            dve.wait_ge(dt_in, 16 * loads)
            for c in range(TC):
                n = min(P, NT - c * P)
                step(nc.vector.tensor_reduce(low[0:n, c, 0:1], dst_t[0:n, c, :], AX, ALU.min))
                step(nc.vector.tensor_reduce(low[0:n, c, 1:2], dst_t[0:n, c, :], AX, ALU.max))
            step(nc.vector.tensor_copy(low_i[:, :, 0:2], low[:, :, :]))
            step(nc.vector.tensor_scalar(low_i[:, :, 2:3], low_i[:, :, 0:1], P - 1, None, ALU.bitwise_and))
            step(nc.vector.tensor_tensor(low[:, :, 1:2], low[:, :, 1:2], low[:, :, 0:1], ALU.subtract))
            step(nc.vector.tensor_copy(low_i[:, :, 3:4], low[:, :, 1:2]))
            step(nc.vector.tensor_scalar(low_i[:, :, 3:4], low_i[:, :, 3:4], 7, None, ALU.arith_shift_right))
            step(nc.vector.tensor_scalar(low_i[:, :, 1:2], low_i[:, :, 0:1], 7, None, ALU.arith_shift_right))
            nc.vector.tensor_copy(bi[:, :, 0:1], low_i[:, :, 1:2])
            nc.vector.tensor_scalar(bi[:, :, 1:2], low_i[:, :, 3:4], 1.0, None, ALU.add).then_inc(bounds_ready, 1)
            nc.vector.tensor_copy(bf[:, :, 1:2], low_i[:, :, 2:3])
            nc.vector.tensor_scalar(bf[:, :, 0:1], low_i[:, :, 1:2], float(P), None, ALU.mult).then_inc(bounds_ready, 1)

            dve.wait_ge(de_in, 32)
            step(nc.vector.tensor_scalar(dst_s, dst_e, P - 1, None, ALU.bitwise_and))
            step(nc.vector.tensor_copy(dparts[:, :, 0:J], dst_s))
            step(nc.vector.tensor_scalar(dst_s, dst_e, 7, None, ALU.arith_shift_right))
            step(nc.vector.tensor_copy(dparts[:, :, J:2 * J], dst_s))

            for b, n in chunks:
                step(dot(b, n, 1, node[:, b:b + n, 0]))
            step(nc.vector.tensor_scalar(node[:, 0:NB, 0], node[:, 0:NB, 0], ba[:, 0:1], None, ALU.add))

            dve.wait_ge(consts, 2)
            step(nc.vector.tensor_copy(pcol[:, :], pcol_i[:, :]))
            step(nc.vector.tensor_copy(wshift[:, :], wcol_i[:, :]))
            step(nc.vector.tensor_scalar(wshift[:, :], wshift[:, :], -P * FAR, None, ALU.mult))
            dve.wait_ge(lowf_in, 16)
            step(nc.vector.tensor_scalar(half[:, :, 1], lowf[:, :, 1], pcol[:, 0:1], None, ALU.is_gt))
            step(nc.vector.tensor_scalar(half[:, :, 0], half[:, :, 1], -1.0, 1.0, ALU.mult, ALU.add))
            step(nc.vector.scalar_tensor_tensor(nidbias[:, :], half[:, :, 1], float(P), lowf[:, :, 0], ALU.mult, ALU.add))
            step(nc.vector.tensor_scalar(nidbias[:, :], nidbias[:, :], pcol[:, 0:1], -FAR, ALU.add, ALU.mult))
            step(nc.vector.tensor_scalar(keep[:, :, :], half[:, :, :], -KEEP, KEEP, ALU.mult, ALU.add))

            dve.wait_ge(wz_copied, 1)
            nc.vector.memset(psG[:, :], 0.0).then_inc(agg_done, 1)
            dve.wait_ge(y_copied, 2 * OCT + 3)
            for i in range(2):
                nc.vector.memset(psT[:, i, :], 0.0).then_inc(tr[i], 1)
            step(nc.vector.memset(acc[:, :], 0.0))

            def edge_product(s):
                return nc.vector.tensor_tensor(prod[:, 0:J * F].rearrange("p (j f) -> p j f", f=F), V[:, s, :, ROW:ROW + F],
                                               wa[:, 2 * F:3 * F].unsqueeze(1).broadcast_to((P, J, F)), ALU.mult)

            def edge_sum():
                return nc.vector.tensor_reduce(q[:, :], prod[:, 0:J * F].rearrange("p (j f) -> p j f", f=F), AX, ALU.add)

            def edge_score(s):
                return nc.vector.tensor_tensor(u[:, :], q[:, :], V[:, s, :, 0], ALU.add)

            dve.wait_ge(ef_in[0], 16)
            step(edge_product(0))
            step(edge_sum())
            dve.wait_ge(h_in[0], 16 * J)
            step(edge_score(0))
            step(nc.vector.tensor_copy(parts[:, 0:J], u[:, :]))
            step(nc.vector.tensor_tensor(urest[:, :], u[:, :], parts[:, 0:J], ALU.subtract))
            step(nc.vector.tensor_copy(parts[:, J:2 * J], urest[:, :]))
            nc.vector.tensor_tensor(parts[:, 2 * J:3 * J], urest[:, :], parts[:, J:2 * J], ALU.subtract)
            nc.vector.tensor_copy(parts[:, 3 * J:5 * J], dparts[:, 0, :]).then_inc(parts_done, 1)
            dve.sem_inc(node_set, 1)
            dve.sem_inc(merged, 1)
            dve.wait_ge(trip_in, 16)

            g = dve.alloc_register("g_dve")
            tp = dve.alloc_register("t_before")
            bp = dve.alloc_register("b_before")
            bn = dve.alloc_register("b_now")
            low_block = dve.alloc_register("low_block")
            count = dve.alloc_register("count_dve")
            coming = [dve.alloc_register("coming_block"), dve.alloc_register("coming_count")]
            dve.load(coming, trip[0:1, 0:2])
            dve.reg_mov(g, 1)
            dve.reg_mov(tp, 0)
            dve.reg_mov(bp, 0)

            def merge(G):
                tb = dve.snap(tp, min_val=0, max_val=NT - 1)
                bb = dve.snap(bp, min_val=0, max_val=NB - 1)
                dve.wait_ge(al_done, G)
                dve.wait_ge(merged, G)
                nc.vector.tensor_tensor(accv[:, bass.ds(bb, 2), :], accv[:, bass.ds(bb, 2), :],
                                        alpha[:, :].unsqueeze(2).broadcast_to((P, 2, AW)), ALU.mult).then_inc(scaled, 1)
                dve.wait_ge(scaled, G)
                dve.wait_ge(agg_done, G)
                for i in range(2):
                    last = nc.vector.scalar_tensor_tensor(accv[:, bass.ds(bb + i, 1), :].rearrange("p a f -> p (a f)"), psG[:, 0:AW],
                                                          half[:, bass.ds(tb, 1), i], accv[:, bass.ds(bb + i, 1), :].rearrange("p a f -> p (a f)"),
                                                          ALU.mult, ALU.add)
                last.then_inc(merged, 1)

            def supertile(k, s, ahead):
                t = RING * k + s
                s1 = (s + 1) % RING
                k1 = k + (1 if s == RING - 1 else 0)
                d = s % 2
                dve.reg_mov(low_block, dve.snap(coming[0]))
                dve.reg_mov(count, dve.snap(coming[1]))
                first = dve.snap(low_block, min_val=0, max_val=NB - 1)
                windows = dve.snap(count, min_val=1, max_val=NB)
                with dve.Fori(0, windows) as w:
                    G = dve.snap(g)
                    dve.reg_mov(bn, first + w)
                    b = dve.snap(bn, min_val=0, max_val=NB - 1)
                    ts = bass.ds(t, 1)
                    nc.vector.tensor_tensor(nbias[:, :], nidbias[:, ts], wshift[:, bass.ds(w, 1)], ALU.add).then_inc(nbias_ready, 1)
                    dve.wait_ge(node_set, G)
                    nc.vector.tensor_scalar(wnode[:, :], node[:, bass.ds(b, 1), :].rearrange("p a k -> p (a k)"), half[:, ts, 0], None, ALU.mult).then_inc(wn0, 1)
                    dve.wait_ge(wn0, G)
                    nc.vector.scalar_tensor_tensor(wnode[:, :], node[:, bass.ds(b + 1, 1), :].rearrange("p a k -> p (a k)"), half[:, ts, 1], wnode[:, :],
                                                   ALU.mult, ALU.add).then_inc(wn1, 1)
                    if ahead:
                        dve.wait_ge(ef_in[s1], 16 * k1 + 16)
                        edge_product(s1).then_inc(prod_done, 1)
                        dve.wait_ge(prod_done, G)
                        edge_sum().then_inc(q_done, 1)
                    dve.wait_ge(u1_copied, 1)
                    dve.wait_ge(sq_done, G)
                    nc.vector.tensor_tensor_reduce(out=um[:, :], in0=ubc[:, d, :], in1=sqd[:, :], scale=1.0, scalar=-3e38,
                                                   op0=ALU.subtract, op1=ALU.max, accum_out=cmax[:, :]).then_inc(cmax_done, 1)
                    if ahead:
                        dve.load(coming, trip[0:1, bass.ds(2 * t + 2, 2)])
                    dve.wait_ge(cmax_done, G)
                    dve.wait_ge(wn1, G)
                    nc.vector.tensor_scalar(nt[:, :], cmax[:, :], wnode[:, 0:1], -1.0, ALU.add, ALU.mult).then_inc(nt_done, 1)
                    dve.wait_ge(nt_done, G)
                    nc.vector.scalar_tensor_tensor(ne[:, :], nt[:, :], SLOPE, nt[:, :], ALU.mult, ALU.min).then_inc(ne_done, 1)
                    dve.wait_ge(ne_done, G)
                    nc.vector.tensor_tensor(nn[:, :], ne[:, :], wnode[:, 1:2], ALU.min).then_inc(nn_done, 1)
                    dve.wait_ge(nn_done, G)
                    nc.vector.tensor_tensor(ebias[:, 0:1], wnode[:, 0:1], nn[:, :], ALU.add)
                    nc.vector.scalar_tensor_tensor(ebias[:, 1:2], wnode[:, 0:1], SLOPE, nn[:, :], ALU.mult, ALU.add).then_inc(m_done, 1)
                    nc.vector.tensor_tensor(dif[:, :], nn[:, :], wnode[:, 1:2], ALU.subtract).then_inc(d_done, 1)
                    nc.vector.scalar_tensor_tensor(node[:, bass.ds(b, 2), 1], keep[:, ts, :].rearrange("p a k -> p (a k)"), nn[:, 0:1], node[:, bass.ds(b, 2), 1],
                                                   ALU.add, ALU.min).then_inc(node_set, 1)
                    if ahead:
                        dve.wait_ge(h_in[s1], 16 * J * k1 + 16 * J)
                        dve.wait_ge(q_done, G)
                        edge_score(s1).then_inc(u_done, 1)
                        dve.wait_ge(u_done, G)
                        dve.wait_ge(tp_done, G)
                        nc.vector.tensor_copy(parts[:, 0:J], u[:, :]).then_inc(p0_done, 1)
                        nc.vector.tensor_copy(parts[:, 3 * J:5 * J], dparts[:, bass.ds(t + 1, 1), :].rearrange("p a k -> p (a k)"))
                        dve.wait_ge(p0_done, G)
                        nc.vector.tensor_tensor(urest[:, :], u[:, :], parts[:, 0:J], ALU.subtract).then_inc(r_done, 1)
                        dve.wait_ge(r_done, G)
                        nc.vector.tensor_copy(parts[:, J:2 * J], urest[:, :]).then_inc(p1_done, 1)
                        dve.wait_ge(p1_done, G)
                        nc.vector.tensor_tensor(parts[:, 2 * J:3 * J], urest[:, :], parts[:, J:2 * J], ALU.subtract).then_inc(parts_done, 1)
                    merge(G)
                    dve.wait_ge(d_done, G)
                    nc.vector.tensor_scalar(dif2[:, :], half[:, ts, :].rearrange("p a k -> p (a k)"), dif[:, 0:1], None, ALU.mult).then_inc(dif_done, 1)
                    dve.wait_ge(e_done, G)
                    nc.vector.tensor_tensor(e1[:, :], e1[:, :], e2[:, :], ALU.max).then_inc(mx_done, 1)
                    dve.reg_mov(tp, t)
                    dve.reg_mov(bp, b)
                    dve.reg_add(g, g, 1)
                dve.sem_inc(v_free[(s - 1) % RING], 1)

            with dve.Fori(0, TURNS) as k:
                for s in range(RING):
                    supertile(k, s, True)
            supertile(TURNS, 0, False)
            last_g = dve.snap(g)
            merge(last_g)
            dve.wait_ge(merged, dve.snap(g) + 1)

            step(nc.vector.tensor_scalar(rl[:, :], accv[:, 0:NB, 2 * F], TINY, None, ALU.max))
            nc.vector.reciprocal(rl[:, :], rl[:, :]).then_inc(all_merged, 1)

            FS = 7

            def finish(o, w):
                b = 8 * o
                blk = bass.ds(b, w)
                rows = y0[:, blk, :]
                base = o * FS
                dve.wait_ge(o_ready, (2 * o + 2) if w == 8 else (2 * o + 1))
                nc.vector.tensor_tensor(rows, rows, psD[:, 0, 0:w * F].rearrange("p (b f) -> p b f", f=F), ALU.add).then_inc(o_read, 1)
                dve.wait_ge(o_read, o + 2)
                prodv = prod[:, 0:w * F].rearrange("p (b f) -> p b f", f=F)
                nc.vector.scalar_tensor_tensor(prodv, rows, 0.0, xt[:, blk, 1:ROW], ALU.max, ALU.add).then_inc(fin_step, 1)
                dve.wait_ge(fin_step, base + 1)
                nc.vector.tensor_reduce(mean[:, 0:w], prodv, AX, ALU.add).then_inc(fin_step, 1)
                dve.wait_ge(fin_step, base + 2)
                nc.vector.tensor_scalar(mean[:, 0:w], mean[:, 0:w], 1.0 / F, None, ALU.mult).then_inc(fin_step, 1)
                dve.wait_ge(fin_step, base + 3)
                nc.vector.tensor_tensor(rows, prodv, mean[:, 0:w].unsqueeze(2).broadcast_to((P, w, F)), ALU.subtract).then_inc(cen_done, 1)
                dve.wait_ge(sq_ready, o + 1)
                nc.vector.tensor_reduce(ssum[:, blk], sqd[:, 0:w * F].rearrange("p (b f) -> p b f", f=F), AX, ALU.add).then_inc(fin_step, FS - 3)

            dve.sem_inc(o_read, 1)
            with dve.Fori(0, OCT) as o:
                finish(o, 8)
            finish(OCT, NR)
            dve.wait_ge(fin_step, FS * (OCT + 1))
            nc.vector.tensor_scalar(ssum[:, :], ssum[:, :], 1.0 / F, EPS, ALU.mult, ALU.add).then_inc(var_ready, 1)
            dve.wait_ge(std_ready, 1)
            step(nc.vector.reciprocal(rstd[:, :], rstd[:, :]))

            def norm(o, w):
                blk = bass.ds(8 * o, w)
                nc.vector.tensor_tensor(y0[:, blk, :], y0[:, blk, :], rstd[:, blk].unsqueeze(2).broadcast_to((P, w, F)), ALU.mult).then_inc(rows_ready, 1)

            with dve.Fori(0, OCT) as o:
                norm(o, 8)
            norm(OCT, NR)

        @block.tensor
        def _(pe):
            pe.wait_ge(pool_step, 11)
            pe.wait_ge(w_in, 16 * 5)
            nc.tensor.transpose(psG[0:F, 0:P], wne[:, :], ident[:, :]).then_inc(wt_ready, 1)
            pe.wait_ge(wt_copied, 1)
            nc.tensor.matmul(psG[:, P:P + F], wneT[:, :], wo_z[:, :], start=True, stop=True).then_inc(wz_ready, 1)

            for c, (b, n) in enumerate(chunks):
                if n > 1 or b + n < NB:
                    pe.wait_ge(x_in[c], 16)
            pe.wait_ge(xr_in, 16)

            def y_turn(n0, g, cnt, b):
                for par in range(cnt):
                    pe.wait_ge(xs_copied, n0 + par + 1)
                    for i in range(g):
                        last = nc.tensor.transpose(psT[0:F, par, i * P:(i + 1) * P], xt[:, b + 4 * par + i, 1:ROW], ident[:, :])
                    last.then_inc(xs_turned, 1)
                for par in range(cnt):
                    pe.wait_ge(xs_copied, n0 + par + 3)
                    pe.wait_ge(y_copied, n0 + par + 1)
                    for i in range(g):
                        last = nc.tensor.matmul(psD[:, par, i * F:(i + 1) * F], e1[0:F, par * 512 + i * P:par * 512 + (i + 1) * P],
                                                wo_x[:, :], start=True, stop=True)
                    last.then_inc(y_ready, 1)

            for o in range(OCT):
                y_turn(2 * o, 4, 2, 8 * o)
            y_turn(2 * OCT, NR, 1, 8 * OCT)

            def stage_b(H, G, d):
                pe.wait_ge(pool_step, 11)
                pe.wait_ge(parts_done, H)
                if G is not None:
                    pe.wait_ge(u1_copied, G)
                nc.tensor.transpose(psTP, parts[:, :], identb[:, :]).then_inc(tp_done, 1)
                pe.wait_ge(tp_copied, H)
                for j in range(4):
                    last = nc.tensor.matmul(psU[:, j * P:(j + 1) * P], sel_u[:, j, :], partsT[:, :], start=True, stop=True)
                last.then_inc(bcu0, 1)
                for j in range(J):
                    last = nc.tensor.matmul(psD[:, d, j * P:(j + 1) * P], sel_d[:, j, :], partsT[:, :], start=True, stop=True)
                last.then_inc(bcd, 1)
                pe.wait_ge(u0_copied, H)
                for j in range(4):
                    last = nc.tensor.matmul(psU[:, j * P:(j + 1) * P], sel_u[:, 4 + j, :], partsT[:, :], start=True, stop=True)
                last.then_inc(bcu1, 1)

            g = pe.alloc_register("g_pe")
            h = pe.alloc_register("h_pe")
            coming = pe.alloc_register("coming_pe")
            count = pe.alloc_register("count_pe")
            pe.reg_mov(g, 1)
            pe.reg_mov(h, 2)
            pe.wait_ge(y_copied, 2 * OCT + 3)
            stage_b(1, None, 0)

            def supertile(t, s, ahead):
                pe.reg_mov(count, pe.snap(coming))
                windows = pe.snap(count, min_val=1, max_val=NB)
                with pe.Fori(0, windows):
                    G, H = pe.snap(g), pe.snap(h)
                    if ahead:
                        stage_b(H, G, 1 - s % 2)
                    pe.wait_ge(mx_done, G)
                    for i in range(2):
                        for j in range(4):
                            last = nc.tensor.transpose(psT[:, i, j * P:(j + 1) * P], e1[:, (4 * i + j) * P:(4 * i + j + 1) * P], ident[:, :])
                        last.then_inc(tr[i], 1)
                    if ahead:
                        pe.load(coming, trip[0:1, bass.ds(2 * t + 3, 1)])
                    for i in range(2):
                        pe.wait_ge(pt[i], H)
                        for j in range(4):
                            last = nc.tensor.matmul(psG[:, 0:AW], pT[:, i, j * P:(j + 1) * P], V[:, s, 4 * i + j, 1:VW],
                                                    start=(i == 0 and j == 0), stop=(i == 1 and j == 3))
                    last.then_inc(agg_done, 1)
                    pe.reg_add(g, g, 1)
                    pe.reg_add(h, h, 1)

            pe.wait_ge(trip_in, 16)
            pe.load(coming, trip[0:1, 1:2])
            with pe.Fori(0, TURNS) as k:
                for s in range(RING):
                    supertile(RING * k + s, s, True)
            supertile(NT - 1, 0, False)

            pe.sem_inc(z_turned, 2)

            def z_turn(n, par, w):
                pe.wait_ge(z_ready, n + 1)
                for i in range(w):
                    last = nc.tensor.transpose(psT[:, par, i * P:(i + 1) * P], e1[:, par * 512 + i * P:par * 512 + (i + 1) * P], ident[:, :])
                last.then_inc(z_turned, 1)

            def z_mul(n, par, w):
                pe.wait_ge(z_copied, n + 1)
                for i in range(w):
                    last = nc.tensor.matmul(psD[:, 0, (4 * par + i) * F:(4 * par + i + 1) * F], pT[:, par, i * P:(i + 1) * P],
                                            wz[:, :], start=True, stop=True)
                last.then_inc(o_ready, 1)

            with pe.Fori(0, OCT) as o:
                for par in range(2):
                    z_turn(2 * o + par, par, 4)
                pe.wait_ge(o_read, o + 1)
                for par in range(2):
                    z_mul(2 * o + par, par, 4)
            z_turn(2 * OCT, 0, NR)
            pe.wait_ge(o_read, OCT + 1)
            z_mul(2 * OCT, 0, NR)


_INS = ['x', 'src', 'dst', 'edge_attr_64', 'L0_gnn_W_ne', 'L0_gnn_W_attn', 'L0_gnn_b_attn', 'L0_gnn_W_out']
_OUTS = [((12500, 64), 'float32')]


def kernel(**inputs):
    import numpy as _np
    import concourse.bacc as _bacc
    from concourse import mybir as _mybir
    from concourse.bass_utils import run_bass_kernel_spmd as _run

    nc = _bacc.Bacc("TRN2", target_bir_lowering=False, num_devices=1)
    arrays, args = {}, []
    for name in _INS:
        a = _np.ascontiguousarray(inputs[name])
        arrays[f"in_{name}_dram"] = a
        args.append(nc.dram_tensor(f"in_{name}_dram", a.shape, _mybir.dt.from_np(a.dtype), kind="ExternalInput").ap())
    for i, (shape, dtype) in enumerate(_OUTS):
        dt = _mybir.dt.from_np(_np.dtype(dtype))
        args.append(nc.dram_tensor(f"out_{i}_dram", shape, dt, kind="ExternalOutput").ap())
    graph_attention(nc, *args)
    r = _run(nc, [arrays], core_ids=[0])
    return r.results[0]["out_0_dram"]
```

```python
from contextlib import ExitStack

import concourse.bass as bass
from concourse import mybir

F32 = mybir.dt.float32
BF16 = mybir.dt.bfloat16
I32 = mybir.dt.int32
U32 = mybir.dt.uint32
ALU = mybir.AluOpType
ACT = mybir.ActivationFunctionType
AX = mybir.AxisListType.X

P = 128
J = 8
ST = P * J
RING = 6
F = 64
ROW = 1 + F
VW = ROW + F + 1
AW = 2 * F + 1
NPART = 5 * J
SLOPE = 0.01
EPS = 1e-5
FAR = 2.0 ** 48
UNSEEN = 1e24
KEEP = 1e30
TINY = 1e-30
CB = 14


def graph_attention(nc, x, src, dst, ef, w_ne, w_att, b_att, w_out, out):
    N, E = x.shape[0], src.shape[0]
    NB = -(-N // P)
    NL = N - (NB - 1) * P
    NT = -(-E // ST)
    PL = (E - (NT - 1) * ST) // J
    TURNS = (NT - 1) // RING
    TC = -(-NT // P)
    OCT = NB // 8
    NR = NB - 8 * OCT
    assert TURNS * RING == NT - 1 and PL * J + (NT - 1) * ST == E
    assert 0 < NR <= 4 and OCT >= 4 and OCT % 2 == 0 and E >= ST
    TABLE = 16 * (-(-NB // CB) + (NB % CB != 1))
    chunks = [(b, min(CB, NB - b)) for b in range(0, NB, CB)]

    ctx = ExitStack()
    with ctx:
        def sb(name, shape, dt=F32):
            return ctx.enter_context(nc.sbuf_tensor(name, shape, dt))

        def ps(name, shape, dt=F32):
            return ctx.enter_context(nc.psum_tensor(name, shape, dt))

        def sem(name):
            return ctx.enter_context(nc.semaphore(name))

        table = nc.dram_tensor("node_table", (N, ROW), F32, kind="Internal").ap()
        bounds_i = nc.dram_tensor("bounds_i", (TC * P, 2), I32, kind="Internal").ap()
        bounds_f = nc.dram_tensor("bounds_f", (TC * P, 2), F32, kind="Internal").ap()

        ident = sb("ident", [P, P])
        identb = sb("identb", [P, P], BF16)
        sel_u = sb("sel_u", [NPART, J, P], BF16)
        sel_d = sb("sel_d", [NPART, J, P], BF16)
        pcol_i = sb("pcol_i", [P, 1], I32)
        pcol = sb("pcol", [P, 1])
        wcol_i = sb("wcol_i", [P, NB + 1], I32)
        wshift = sb("wshift", [P, NB + 1])
        wa = sb("wa", [P, 3 * F])
        ba = sb("ba", [P, 1])
        wne = sb("wne", [P, F])
        wneT = sb("wneT", [F, P])
        wo_x = sb("wo_x", [F, F])
        wo_z = sb("wo_z", [F, F])
        wz = sb("wz", [P, F])
        xt = sb("xt", [P, NB, ROW])
        y0 = sb("y0", [P, NB, F])
        acc = sb("acc", [P, (NB + 1) * AW])
        accv = acc[:, :].rearrange("p (b f) -> p b f", f=AW)
        node = sb("node", [P, NB + 1, 2])
        V = sb("V", [P, RING, J, VW])
        srcs = sb("srcs", [P, RING, J], U32)
        dparts = sb("dparts", [P, NT, 2 * J], BF16)
        trip = sb("trip", [1, TC * P * 2], I32)
        lowf = sb("lowf", [P, NT, 2])
        nidbias = sb("nidbias", [P, NT])
        half = sb("half", [P, NT, 2])
        keep = sb("keep", [P, NT, 2])
        low = sb("low", [P, TC, 2])
        low_i = sb("low_i", [P, TC, 4], I32)
        bi = sb("bi", [P, TC, 2], I32)
        bf = sb("bf", [P, TC, 2])
        prod = sb("prod", [P, 1024])
        q = sb("q", [P, 2, J])
        u = sb("u", [P, J])
        urest = sb("urest", [P, J])
        parts = sb("parts", [P, NPART], BF16)
        partsT = sb("partsT", [NPART, P], BF16)
        ubc = sb("ubc", [P, 2, ST])
        sqd = sb("sqd", [P, ST])
        um = sb("um", [P, ST])
        e1 = sb("e1", [P, ST])
        e2 = sb("e2", [P, ST])
        pT = sb("pT", [P, 2, 512])
        nbias = sb("nbias", [P, 1])
        wnode = sb("wnode", [P, 2])
        cmax = sb("cmax", [P, 1])
        nt = sb("nt", [P, 1])
        ne = sb("ne", [P, 1])
        nn = sb("nn", [P, 1])
        ebias = sb("ebias", [P, 2])
        dif = sb("dif", [P, 1])
        dif2 = sb("dif2", [P, 2])
        alpha = sb("alpha", [P, 2])
        rl = sb("rl", [P, NB])
        mean = sb("mean", [P, 8])
        var = sb("var", [P, NB])
        rstd = sb("rstd", [P, NB])

        raw = acc[:, :].bitcast(I32)
        dst_e = raw[:, 0:NT * J].rearrange("p (t j) -> p t j", j=J)
        dst_s = raw[:, NT * J:2 * NT * J].rearrange("p (t j) -> p t j", j=J)
        dst_t = raw[:, 2 * NT * J:2 * NT * J + TC * ST].rearrange("p (c e) -> p c e", c=TC)

        psU = ps("psU", [P, 512])
        psTP = psU[0:NPART, 0:P // 2].bitcast(BF16)
        psD = ps("psD", [P, 2, ST])
        psT = ps("psT", [P, 2, 512])
        psG = ps("psG", [P, 512])

        w_in = sem("w_in")
        x_in = [sem(f"x_in{c}") for c in range(len(chunks))]
        xr_in = sem("xr_in")
        dt_in = sem("dt_in")
        de_in = sem("de_in")
        idx_in = [sem(f"idx_in{s}") for s in range(RING)]
        ef_in = [sem(f"ef_in{s}") for s in range(RING)]
        h_in = [sem(f"h_in{s}") for s in range(RING)]
        table_out = sem("table_out")
        bounds_out = sem("bounds_out")
        trip_in = sem("trip_in")
        lowf_in = sem("lowf_in")
        out_done = sem("out_done")
        pool_step = sem("pool_step")
        consts = sem("consts")
        dve_step = sem("dve_step")
        xpad = sem("xpad")
        dpad = sem("dpad")
        dst_used = sem("dst_used")
        acc_cleared = sem("acc_cleared")
        as_ready = sem("as_ready")
        bounds_ready = sem("bounds_ready")
        wt_ready = sem("wt_ready")
        wt_copied = sem("wt_copied")
        wz_ready = sem("wz_ready")
        wz_copied = sem("wz_copied")
        xs_turned = sem("xs_turned")
        xs_copied = sem("xs_copied")
        y_ready = sem("y_ready")
        y_copied = sem("y_copied")
        v_free = [sem(f"v_free{s}") for s in range(RING)]
        nbias_ready = sem("nbias_ready")
        sq_done = sem("sq_done")
        m_done = sem("m_done")
        e_done = sem("e_done")
        mx_done = sem("mx_done")
        dif_done = sem("dif_done")
        al_done = sem("al_done")
        parts_done = sem("parts_done")
        tp_done = sem("tp_done")
        tp_copied = sem("tp_copied")
        bcu0 = sem("bcu0")
        bcu1 = sem("bcu1")
        bcd = sem("bcd")
        u0_copied = sem("u0_copied")
        u1_copied = sem("u1_copied")
        tr = [sem("tr0"), sem("tr1")]
        pt = [sem("pt0"), sem("pt1")]
        agg_done = sem("agg_done")
        merged = sem("merged")
        node_set = sem("node_set")
        wn0 = sem("wn0")
        wn1 = sem("wn1")
        prod_done = sem("prod_done")
        q_done = sem("q_done")
        cmax_done = sem("cmax_done")
        nt_done = sem("nt_done")
        ne_done = sem("ne_done")
        nn_done = sem("nn_done")
        d_done = sem("d_done")
        scaled = sem("scaled")
        u_done = sem("u_done")
        r_done = sem("r_done")
        p1_done = sem("p1_done")
        all_merged = sem("all_merged")
        z_ready = sem("z_ready")
        z_turned = sem("z_turned")
        z_copied = sem("z_copied")
        o_ready = sem("o_ready")
        o_read = sem("o_read")
        cen_done = sem("cen_done")
        relu_done = sem("relu_done")
        sum_done = sem("sum_done")
        sq_ready = sem("sq_ready")
        sq_summed = sem("sq_summed")
        var_done = sem("var_done")
        std_ready = sem("std_ready")
        rstd_done = sem("rstd_done")
        rows_ready = sem("rows_ready")

        def width(o):
            return 8 if not isinstance(o, int) or 0 <= o < OCT else NR if o == OCT else 0

        def octets(engine, octet, late):
            for o in range(4):
                octet(o, o % 2)
            with engine.Fori(2, OCT // 2) if OCT > 4 else ExitStack() as i:
                if OCT > 4:
                    octet(2 * i, 0)
                    octet(2 * i + 1, 1)
            for o in range(max(4, OCT), OCT + 1 + late):
                octet(o, o % 2)

        block = ctx.enter_context(nc.Block())

        def edge_rows(dram, t):
            return dram[bass.ds(t * ST, ST)] if not isinstance(t, int) else dram[t * ST:(t + 1) * ST]

        @block.sync
        def _(sp):
            sp.dma_start(wa[:, :], w_att.rearrange("a b -> b a").broadcast_to((P, 3 * F))).then_inc(w_in, 16)
            sp.dma_start(ba[:, :], b_att.rearrange("(a b) -> a b", a=1).broadcast_to((P, 1))).then_inc(w_in, 16)
            sp.dma_start(wne[:, :], w_ne[:, :]).then_inc(w_in, 16)
            sp.dma_start(wo_x[:, :], w_out[0:F, :]).then_inc(w_in, 16)
            sp.dma_start(wo_z[:, :], w_out[F:2 * F, :]).then_inc(w_in, 16)
            full = NT - 1
            for c in range(TC):
                n = min(P, full - c * P)
                if n > 0:
                    sp.dma_start(dst_t[0:n, c, :], dst[c * ST * P:c * ST * P + n * ST].rearrange("(p e) -> p e", e=ST)).then_inc(dt_in, 16)
            pl = full - (TC - 1) * P
            sp.dma_start(dst_t[pl:pl + 1, TC - 1, :], dst[E - ST:E].rearrange("(p e) -> p e", e=ST)).then_inc(dt_in, 16)
            sp.wait_ge(dpad, 1)
            sp.dma_start(dst_e[:, 0:full, :], dst[0:full * ST].rearrange("(t p j) -> p t j", p=P, j=J)).then_inc(de_in, 16)
            sp.dma_start(dst_e[0:PL, full, :], dst[full * ST:E].rearrange("(p j) -> p j", j=J)).then_inc(de_in, 16)

            def load(t, s):
                sp.dma_start(srcs[:, s, :], edge_rows(src, t).rearrange("(p j) -> p j", j=J).bitcast(U32)).then_inc(idx_in[s], 16)
                sp.dma_start(V[:, s, :, ROW:ROW + F], (ef[bass.ds(t * ST, ST), :]).rearrange("(p j) f -> p j f", j=J)).then_inc(ef_in[s], 16)

            for s in range(2):
                load(s, s)
            for c, (b, n) in enumerate(chunks):
                last = b + n == NB
                m = n - 1 if last else n
                sp.wait_ge(as_ready, c + 1)
                if m:
                    sp.dma_start(table[b * P:(b + m) * P, :].rearrange("(b p) f -> p b f", p=P), xt[:, b:b + m, :]).then_inc(table_out, 16)
                if last:
                    sp.dma_start(table[(NB - 1) * P:N, :], xt[0:NL, NB - 1, :]).then_inc(table_out, 16)
            for s in range(2, RING):
                load(s, s)
            sp.wait_ge(bounds_ready, 2)
            sp.dma_start(bounds_i.rearrange("(c p) k -> p c k", p=P), bi[:, :, :]).then_inc(bounds_out, 16)
            sp.dma_start(bounds_f.rearrange("(c p) k -> p c k", p=P), bf[:, :, :]).then_inc(bounds_out, 16)
            sp.wait_ge(bounds_out, 32)
            sp.dma_start(trip[:, :], bounds_i.rearrange("t k -> (t k)").rearrange("(a b) -> a b", a=1)).then_inc(trip_in, 16)
            sp.dma_start(lowf[:, :, :], bounds_f[0:NT, :].rearrange("t k -> (t k)").rearrange("(a b) -> a b", a=1).broadcast_to((P, NT * 2)).rearrange("p (t k) -> p t k", k=2)).then_inc(lowf_in, 16)
            with sp.Fori(1, TURNS) if TURNS > 1 else ExitStack() as k:
                if TURNS > 1:
                    for s in range(RING):
                        sp.wait_ge(v_free[s], k + (1 if s >= RING - 2 else 0))
                        load(RING * k + s, s)
            sp.wait_ge(v_free[0], TURNS)
            sp.dma_start(srcs[0:PL, 0, :], src[full * ST:E].rearrange("(p j) -> p j", j=J).bitcast(U32)).then_inc(idx_in[0], 16)
            sp.dma_start(V[0:PL, 0, :, ROW:ROW + F], ef[full * ST:E, :].rearrange("(p j) f -> p j f", j=J)).then_inc(ef_in[0], 16)
            sp.wait_ge(v_free[1], TURNS)
            sp.dma_start(V[:, 1, :, ROW:ROW + F], ef[0:ST, :].rearrange("(p j) f -> p j f", j=J)).then_inc(ef_in[1], 16)
            for o in range(OCT):
                sp.wait_ge(rows_ready, o + 1)
                sp.dma_start(out[o * 8 * P:(o + 1) * 8 * P, :].rearrange("(b p) f -> p b f", p=P), y0[:, 8 * o:8 * o + 8, :]).then_inc(out_done, 16)
            sp.wait_ge(rows_ready, OCT + 1)
            n = NR - 1
            outs = OCT + 1
            if n:
                sp.dma_start(out[8 * OCT * P:(NB - 1) * P, :].rearrange("(b p) f -> p b f", p=P), y0[:, 8 * OCT:NB - 1, :]).then_inc(out_done, 16)
                outs += 1
            sp.dma_start(out[(NB - 1) * P:N, :], y0[0:NL, NB - 1, :]).then_inc(out_done, 16)
            sp.wait_ge(out_done, 16 * outs)

        @block.gpsimd
        def _(pool):
            step = 0
            for ap in (ident[:, :], identb[:, :], sel_u[:, :, :], sel_d[:, :, :]):
                nc.gpsimd.memset(ap, 0.0).then_inc(pool_step, 1)
                step += 1
            pool.wait_ge(pool_step, step)
            for t_ in (ident, identb):
                nc.gpsimd.affine_select(out=t_[:, :], in_=t_[:, :], compare_op=ALU.not_equal, fill=1.0, base=0,
                                        pattern=[[-1, P]], channel_multiplier=1).then_inc(pool_step, 1)
                step += 1
            for t_, row, fill in ((sel_u, 0, 1.0), (sel_u, J, 1.0), (sel_u, 2 * J, 1.0),
                                  (sel_d, 3 * J, 1.0), (sel_d, 4 * J, float(P))):
                nc.gpsimd.affine_select(out=t_[:, :, :], in_=t_[:, :, :], compare_op=ALU.not_equal, fill=fill,
                                        base=-row, pattern=[[-1, J], [0, P]], channel_multiplier=1).then_inc(pool_step, 1)
                step += 1
                pool.wait_ge(pool_step, step)
            nc.gpsimd.iota(pcol_i[:, :], pattern=[[0, 1]], base=0, channel_multiplier=1).then_inc(consts, 1)
            nc.gpsimd.iota(wcol_i[:, :], pattern=[[1, NB + 1]], base=0, channel_multiplier=0).then_inc(consts, 1)

            def gather(s, n):
                for j in range(J):
                    nc.gpsimd.indirect_dma_start(V[0:n, s, j, 0:ROW], None, table[:, :],
                                                 bass.IndirectOffsetOnAxis(ap=srcs[0:n, s, j:j + 1], axis=0)).then_inc(h_in[s], 16)

            pool.wait_ge(table_out, TABLE)
            for s in range(RING):
                pool.wait_ge(idx_in[s], 16)
                gather(s, P)
            if TURNS > 1:
                arrived, freed_last = pool.alloc_register("arrived"), pool.alloc_register("freed_last")
                with pool.Fori(1, TURNS) as k:
                    pool.reg_mov(arrived, 16 * k + 16)
                    pool.reg_mov(freed_last, k + 1)
                    indices = pool.snap(arrived)
                    for s in range(RING):
                        freed = k if s < RING - 2 else pool.snap(freed_last)
                        pool.wait_ge(table_out, TABLE)
                        pool.wait_ge(idx_in[s], indices)
                        pool.wait_ge(v_free[s], freed)
                        gather(s, P)
            pool.wait_ge(idx_in[0], 16 * TURNS + 16)
            pool.wait_ge(v_free[0], TURNS)
            gather(0, PL)

            pool.wait_ge(all_merged, 1)

            def octet(o, par):
                w = width(o)
                pool.wait_ge(z_turned, 2 * o + 2)
                nc.gpsimd.tensor_tensor((e1, e2)[par][:, 0:w * P].rearrange("p (b f) -> p b f", f=P), accv[:, bass.ds(8 * o, w), 0:P],
                                        rl[:, bass.ds(8 * o, w)].unsqueeze(2).broadcast_to((P, w, P)), ALU.mult).then_inc(z_ready, 1)

            octets(pool, octet, 0)

        @block.scalar
        def _(act):
            for c, (b, n) in enumerate(chunks):
                last = b + n == NB
                m = n - 1 if last else n
                if last:
                    act.wait_ge(xpad, 1)
                if m:
                    act.dma_start(xt[:, b:b + m, 1:ROW], x[b * P:(b + m) * P, :].rearrange("(b p) f -> p b f", p=P)).then_inc(x_in[c], 16)
                if last:
                    act.dma_start(xt[0:NL, NB - 1, 1:ROW], x[(NB - 1) * P:N, :]).then_inc(xr_in, 16)
            act.sem_inc(xs_copied, 2)
            act.sem_inc(y_copied, 2)
            act.wait_ge(wt_ready, 1)
            nc.scalar.copy(wneT[:, :], psG[0:F, 0:P]).then_inc(wt_copied, 1)
            act.wait_ge(wz_ready, 1)
            nc.scalar.copy(wz[:, :], psG[:, P:P + F]).then_inc(wz_copied, 1)

            def y_turn(n0, g, cnt, b):
                for par in range(cnt):
                    w = g if cnt == 1 else 4
                    act.wait_ge(xs_turned, n0 + par + 1)
                    nc.scalar.copy(e1[0:F, par * 512:par * 512 + w * P], psT[0:F, par, 0:w * P]).then_inc(xs_copied, 1)
                for par in range(cnt):
                    w = g if cnt == 1 else 4
                    act.wait_ge(y_ready, n0 + par + 1)
                    dst_ap = y0[:, b + 4 * par:b + 4 * par + w, :] if isinstance(b, int) else y0[:, bass.ds(b + 4 * par, w), :]
                    nc.scalar.copy(dst_ap, psD[:, par, 0:w * F].rearrange("p (b f) -> p b f", f=F)).then_inc(y_copied, 1)

            with act.Fori(0, OCT) as o:
                y_turn(2 * o, 4, 2, 8 * o)
            y_turn(2 * OCT, NR, 1, 8 * OCT)

            act.wait_ge(dst_used, 1)
            nc.scalar.copy(acc[:, 0:NT * J], acc[:, 2 * NT * J:3 * NT * J]).then_inc(acc_cleared, 1)

            def parts_out(H):
                act.wait_ge(tp_done, H)
                nc.scalar.copy(partsT[:, :], psTP).then_inc(tp_copied, 1)

            def scores_out(H, d, i):
                act.wait_ge((bcu0, bcu1)[i], H)
                nc.scalar.copy(ubc[:, d, 512 * i:512 * i + 512], psU[:, :]).then_inc((u0_copied, u1_copied)[i], 1)

            g = act.alloc_register("g_act")
            h = act.alloc_register("h_act")
            coming = act.alloc_register("coming_act")
            count = act.alloc_register("count_act")
            act.reg_mov(g, 1)
            act.reg_mov(h, 2)
            parts_out(1)
            scores_out(1, 0, 0)
            scores_out(1, 0, 1)

            def weights_out(G, i):
                act.wait_ge(tr[i], G)
                nc.scalar.copy(pT[:, i, :], psT[:, i, :]).then_inc(pt[i], 1)

            def supertile(t, s, ahead):
                act.reg_mov(count, act.snap(coming))
                windows = act.snap(count, min_val=1, max_val=NB)
                d = s % 2
                if not ahead:
                    act.wait_ge(bcd, act.snap(g))
                with act.Fori(0, windows):
                    G, H = act.snap(g), act.snap(h)
                    if ahead:
                        act.wait_ge(bcd, G)
                    act.wait_ge(nbias_ready, G)
                    nc.scalar.activation(sqd[:, :], psD[:, d, :], ACT.Square, bias=nbias[:, 0:1], scale=FAR).then_inc(sq_done, 1)
                    weights_out(G, 0)
                    if ahead:
                        parts_out(H)
                    weights_out(G, 1)
                    if ahead:
                        scores_out(H, 1 - d, 0)
                    act.wait_ge(m_done, G)
                    nc.scalar.activation(e1[:, :], um[:, :], ACT.Exp, bias=ebias[:, 0:1])
                    nc.scalar.activation(e2[:, :], um[:, :], ACT.Exp, bias=ebias[:, 1:2], scale=SLOPE).then_inc(e_done, 1)
                    if ahead:
                        act.load(coming, trip[0:1, bass.ds(2 * t + 3, 1)])
                        scores_out(H, 1 - d, 1)
                    act.wait_ge(dif_done, G)
                    nc.scalar.activation(alpha[:, :], dif2[:, :], ACT.Exp).then_inc(al_done, 1)
                    act.reg_add(g, g, 1)
                    act.reg_add(h, h, 1)

            act.wait_ge(trip_in, 16)
            act.load(coming, trip[0:1, 1:2])
            with act.Fori(0, TURNS) as k:
                for s in range(RING):
                    supertile(RING * k + s, s, True)
            supertile(NT - 1, 0, False)
            weights_out(act.snap(g), 0)
            weights_out(act.snap(g), 1)

            act.sem_inc(z_copied, 2)

            def octet(o, par):
                w, w1, w3 = width(o), width(o - 1), width(o - 3)
                if w3:
                    blk3 = bass.ds(8 * (o - 3), w3)
                    act.wait_ge(var_done, o - 2)
                    nc.scalar.activation(rstd[:, blk3], var[:, blk3], ACT.Sqrt).then_inc(std_ready, 1)
                for i in range(-(-w // 4)):
                    m = min(4, w - 4 * i)
                    act.wait_ge(z_turned, 2 * o + i + 5)
                    if i == 0:
                        act.wait_ge(o_ready, o + 1)
                    nc.scalar.copy(ubc[:, par, 512 * i:512 * i + m * P], psT[:, i, 0:m * P]).then_inc(z_copied, 1)
                if w1:
                    act.wait_ge(cen_done, o)
                    nc.scalar.activation((sqd, um)[1 - par][:, 0:w1 * F].rearrange("p (b f) -> p b f", f=F), y0[:, bass.ds(8 * (o - 1), w1), :],
                                         ACT.Square).then_inc(sq_ready, 1)

            octets(act, octet, 3)

        @block.vector
        def _(dve):
            steps = [0]

            def step(ins):
                steps[0] += 1
                ins.then_inc(dve_step, 1)
                dve.wait_ge(dve_step, steps[0])

            nc.vector.memset(xt[:, NB - 1, :], 0.0).then_inc(xpad, 1)
            nc.vector.memset(dst_e[:, NT - 1, :], -P).then_inc(dpad, 1)
            nc.vector.memset(V[:, :, :, VW - 1:VW], 1.0)
            nc.vector.memset(node[:, :, 1:2], UNSEEN)
            nc.vector.memset(node[:, NB:NB + 1, 0:1], 0.0)
            nc.vector.memset(alpha[:, :], 1.0).then_inc(al_done, 1)
            nc.vector.memset(dif2[:, :], 0.0)
            nc.vector.memset(low[:, :, :], 0.0)
            step(nc.vector.memset(q[:, :, :], 0.0))
            dve.wait_ge(w_in, 16 * 5)

            def dot(b, n, w, dest):
                step(nc.vector.tensor_tensor(prod[:, 0:n * F].rearrange("p (b f) -> p b f", f=F), xt[:, b:b + n, 1:ROW],
                                             wa[:, w * F:(w + 1) * F].unsqueeze(1).broadcast_to((P, n, F)), ALU.mult))
                return nc.vector.tensor_reduce(dest, prod[:, 0:n * F].rearrange("p (b f) -> p b f", f=F), AX, ALU.add)

            for c, (b, n) in enumerate(chunks):
                if n > 1 or b + n < NB:
                    dve.wait_ge(x_in[c], 16)
                if b + n == NB:
                    dve.wait_ge(xr_in, 16)
                dot(b, n, 0, xt[:, b:b + n, 0]).then_inc(as_ready, 1)
                dve.wait_ge(as_ready, c + 1)

            loads = sum(1 for c in range(TC) if min(P, NT - 1 - c * P) > 0) + 1
            dve.wait_ge(dt_in, 16 * loads)
            for c in range(TC):
                n = min(P, NT - c * P)
                step(nc.vector.tensor_reduce(low[0:n, c, 0:1], dst_t[0:n, c, :], AX, ALU.min))
                step(nc.vector.tensor_reduce(low[0:n, c, 1:2], dst_t[0:n, c, :], AX, ALU.max))
            step(nc.vector.tensor_copy(low_i[:, :, 0:2], low[:, :, :]))
            step(nc.vector.tensor_scalar(low_i[:, :, 2:3], low_i[:, :, 0:1], P - 1, None, ALU.bitwise_and))
            step(nc.vector.tensor_tensor(low[:, :, 1:2], low[:, :, 1:2], low[:, :, 0:1], ALU.subtract))
            step(nc.vector.tensor_copy(low_i[:, :, 3:4], low[:, :, 1:2]))
            step(nc.vector.tensor_scalar(low_i[:, :, 3:4], low_i[:, :, 3:4], 7, None, ALU.arith_shift_right))
            step(nc.vector.tensor_scalar(low_i[:, :, 1:2], low_i[:, :, 0:1], 7, None, ALU.arith_shift_right))
            nc.vector.tensor_copy(bi[:, :, 0:1], low_i[:, :, 1:2])
            nc.vector.tensor_scalar(bi[:, :, 1:2], low_i[:, :, 3:4], 1.0, None, ALU.add).then_inc(bounds_ready, 1)
            nc.vector.tensor_copy(bf[:, :, 1:2], low_i[:, :, 2:3])
            nc.vector.tensor_scalar(bf[:, :, 0:1], low_i[:, :, 1:2], float(P), None, ALU.mult).then_inc(bounds_ready, 1)

            for b, n in chunks:
                step(dot(b, n, 1, node[:, b:b + n, 0]))
            step(nc.vector.tensor_scalar(node[:, 0:NB, 0], node[:, 0:NB, 0], ba[:, 0:1], None, ALU.add))

            nc.vector.memset(acc[:, 2 * NT * J:], 0.0)
            dve.wait_ge(de_in, 32)
            step(nc.vector.tensor_scalar(dst_s, dst_e, P - 1, None, ALU.bitwise_and))
            step(nc.vector.tensor_copy(dparts[:, :, 0:J], dst_s))
            step(nc.vector.tensor_scalar(dst_s, dst_e, 7, None, ALU.arith_shift_right))
            dve.sem_inc(dst_used, 1)
            step(nc.vector.tensor_copy(dparts[:, :, J:2 * J], dst_s))

            dve.wait_ge(consts, 2)
            step(nc.vector.tensor_copy(pcol[:, :], pcol_i[:, :]))
            step(nc.vector.tensor_copy(wshift[:, :], wcol_i[:, :]))
            step(nc.vector.tensor_scalar(wshift[:, :], wshift[:, :], -P * FAR, None, ALU.mult))
            dve.wait_ge(lowf_in, 16)
            step(nc.vector.tensor_scalar(half[:, :, 1], lowf[:, :, 1], pcol[:, 0:1], None, ALU.is_gt))
            step(nc.vector.tensor_scalar(half[:, :, 0], half[:, :, 1], -1.0, 1.0, ALU.mult, ALU.add))
            step(nc.vector.scalar_tensor_tensor(nidbias[:, :], half[:, :, 1], float(P), lowf[:, :, 0], ALU.mult, ALU.add))
            step(nc.vector.tensor_scalar(nidbias[:, :], nidbias[:, :], pcol[:, 0:1], -FAR, ALU.add, ALU.mult))
            step(nc.vector.tensor_scalar(keep[:, :, :], half[:, :, :], -KEEP, KEEP, ALU.mult, ALU.add))

            dve.wait_ge(wz_copied, 1)
            nc.vector.memset(psG[:, :], 0.0).then_inc(agg_done, 1)
            nc.vector.memset(acc[:, NT * J:2 * NT * J], 0.0)

            def edge_product(s):
                return nc.vector.tensor_tensor(prod[:, 0:J * F].rearrange("p (j f) -> p j f", f=F), V[:, s, :, ROW:ROW + F],
                                               wa[:, 2 * F:3 * F].unsqueeze(1).broadcast_to((P, J, F)), ALU.mult)

            def edge_sum(i):
                return nc.vector.tensor_reduce(q[:, i, :], prod[:, 0:J * F].rearrange("p (j f) -> p j f", f=F), AX, ALU.add)

            def edge_score(dest, i, s):
                return nc.vector.tensor_tensor(dest, q[:, i, :], V[:, s, :, 0], ALU.add)

            dve.wait_ge(ef_in[0], 16)
            step(edge_product(0))
            step(edge_sum(0))
            dve.wait_ge(h_in[0], 16 * J)
            edge_score(parts[:, 0:J], 0, 0)
            step(edge_score(u[:, :], 0, 0))
            step(nc.vector.tensor_tensor(urest[:, :], u[:, :], parts[:, 0:J], ALU.subtract))
            step(nc.vector.tensor_copy(parts[:, J:2 * J], urest[:, :]))
            nc.vector.tensor_tensor(parts[:, 2 * J:3 * J], urest[:, :], parts[:, J:2 * J], ALU.subtract)
            nc.vector.tensor_copy(parts[:, 3 * J:5 * J], dparts[:, 0, :]).then_inc(parts_done, 1)
            dve.wait_ge(ef_in[1], 16)
            step(edge_product(1))
            step(edge_sum(1))
            dve.wait_ge(y_copied, 2 * OCT + 3)
            for i in range(2):
                nc.vector.memset(psT[:, i, :], 0.0).then_inc(tr[i], 1)
            dve.wait_ge(acc_cleared, 1)
            dve.sem_inc(node_set, 1)
            dve.sem_inc(scaled, 1)
            dve.wait_ge(trip_in, 16)

            g = dve.alloc_register("g_dve")
            t1 = dve.alloc_register("t_before")
            b1 = dve.alloc_register("b_before")
            t2 = dve.alloc_register("t_two_before")
            b2 = dve.alloc_register("b_two_before")
            bn = dve.alloc_register("b_now")
            low_block = dve.alloc_register("low_block")
            count = dve.alloc_register("count_dve")
            coming = [dve.alloc_register("coming_block"), dve.alloc_register("coming_count")]
            dve.load(coming, trip[0:1, 0:2])
            dve.reg_mov(g, 1)
            for r in (t1, b1, t2, b2):
                dve.reg_mov(r, 0)

            def rescale(G):
                bb = dve.snap(b1, min_val=0, max_val=NB - 1)
                dve.wait_ge(al_done, G)
                dve.wait_ge(merged, G)
                nc.vector.tensor_tensor(accv[:, bass.ds(bb, 2), :], accv[:, bass.ds(bb, 2), :],
                                        alpha[:, :].unsqueeze(2).broadcast_to((P, 2, AW)), ALU.mult).then_inc(scaled, 1)

            def merge(G):
                tb = dve.snap(t2, min_val=0, max_val=NT - 1)
                bb = dve.snap(b2, min_val=0, max_val=NB - 1)
                dve.wait_ge(scaled, G)
                dve.wait_ge(agg_done, G)
                for i in range(2):
                    row = accv[:, bass.ds(bb + i, 1), :].rearrange("p a f -> p (a f)")
                    last = nc.vector.scalar_tensor_tensor(row, psG[:, 0:AW], half[:, bass.ds(tb, 1), i], row, ALU.mult, ALU.add)
                last.then_inc(merged, 1)

            def supertile(k, s, ahead):
                t = RING * k + s
                s1, s2 = (s + 1) % RING, (s + 2) % RING
                k1, k2 = k + (s + 1) // RING, k + (s + 2) // RING
                d = s % 2
                dve.reg_mov(low_block, dve.snap(coming[0]))
                dve.reg_mov(count, dve.snap(coming[1]))
                first = dve.snap(low_block, min_val=0, max_val=NB - 1)
                windows = dve.snap(count, min_val=1, max_val=NB)
                with dve.Fori(0, windows) as w:
                    G = dve.snap(g)
                    dve.reg_mov(bn, first + w)
                    b = dve.snap(bn, min_val=0, max_val=NB - 1)
                    ts = bass.ds(t, 1)
                    nc.vector.tensor_tensor(nbias[:, :], nidbias[:, ts], wshift[:, bass.ds(w, 1)], ALU.add).then_inc(nbias_ready, 1)
                    dve.wait_ge(node_set, G)
                    nc.vector.tensor_scalar(wnode[:, :], node[:, bass.ds(b, 1), :].rearrange("p a k -> p (a k)"), half[:, ts, 0], None, ALU.mult).then_inc(wn0, 1)
                    if ahead:
                        dve.wait_ge(h_in[s1], 16 * J * k1 + 16 * J)
                        dve.wait_ge(tp_done, G)
                        edge_score(u[:, :], 1 - d, s1)
                        edge_score(parts[:, 0:J], 1 - d, s1).then_inc(u_done, 1)
                    dve.wait_ge(wn0, G)
                    nc.vector.scalar_tensor_tensor(wnode[:, :], node[:, bass.ds(b + 1, 1), :].rearrange("p a k -> p (a k)"), half[:, ts, 1], wnode[:, :],
                                                   ALU.mult, ALU.add).then_inc(wn1, 1)
                    if ahead:
                        dve.wait_ge(u_done, G)
                        nc.vector.tensor_tensor(urest[:, :], u[:, :], parts[:, 0:J], ALU.subtract).then_inc(r_done, 1)
                        nc.vector.tensor_copy(parts[:, 3 * J:5 * J], dparts[:, bass.ds(t + 1, 1), :].rearrange("p a k -> p (a k)"))
                        dve.wait_ge(r_done, G)
                        nc.vector.tensor_copy(parts[:, J:2 * J], urest[:, :]).then_inc(p1_done, 1)
                        dve.wait_ge(p1_done, G)
                        nc.vector.tensor_tensor(parts[:, 2 * J:3 * J], urest[:, :], parts[:, J:2 * J], ALU.subtract).then_inc(parts_done, 1)
                    merge(G)
                    dve.wait_ge(u1_copied, 1)
                    dve.wait_ge(sq_done, G)
                    nc.vector.tensor_tensor_reduce(out=um[:, :], in0=ubc[:, d, :], in1=sqd[:, :], scale=1.0, scalar=-3e38,
                                                   op0=ALU.subtract, op1=ALU.max, accum_out=cmax[:, :]).then_inc(cmax_done, 1)
                    if ahead:
                        dve.load(coming, trip[0:1, bass.ds(2 * t + 2, 2)])
                    dve.wait_ge(cmax_done, G)
                    dve.wait_ge(wn1, G)
                    nc.vector.tensor_scalar(nt[:, :], cmax[:, :], wnode[:, 0:1], -1.0, ALU.add, ALU.mult).then_inc(nt_done, 1)
                    dve.wait_ge(nt_done, G)
                    nc.vector.scalar_tensor_tensor(ne[:, :], nt[:, :], SLOPE, nt[:, :], ALU.mult, ALU.min).then_inc(ne_done, 1)
                    dve.wait_ge(ne_done, G)
                    nc.vector.tensor_tensor(nn[:, :], ne[:, :], wnode[:, 1:2], ALU.min).then_inc(nn_done, 1)
                    dve.wait_ge(nn_done, G)
                    nc.vector.tensor_tensor(ebias[:, 0:1], wnode[:, 0:1], nn[:, :], ALU.add)
                    nc.vector.scalar_tensor_tensor(ebias[:, 1:2], wnode[:, 0:1], SLOPE, nn[:, :], ALU.mult, ALU.add).then_inc(m_done, 1)
                    nc.vector.tensor_tensor(dif[:, :], nn[:, :], wnode[:, 1:2], ALU.subtract).then_inc(d_done, 1)
                    nc.vector.scalar_tensor_tensor(node[:, bass.ds(b, 2), 1], keep[:, ts, :].rearrange("p a k -> p (a k)"), nn[:, 0:1], node[:, bass.ds(b, 2), 1],
                                                   ALU.add, ALU.min).then_inc(node_set, 1)
                    rescale(G)
                    dve.wait_ge(d_done, G)
                    nc.vector.tensor_scalar(dif2[:, :], half[:, ts, :].rearrange("p a k -> p (a k)"), dif[:, 0:1], None, ALU.mult).then_inc(dif_done, 1)
                    if ahead:
                        dve.wait_ge(ef_in[s2], 16 * k2 + 16)
                        edge_product(s2).then_inc(prod_done, 1)
                        dve.wait_ge(prod_done, G)
                        edge_sum(d).then_inc(q_done, 1)
                    dve.wait_ge(e_done, G)
                    nc.vector.tensor_tensor(e1[:, :], e1[:, :], e2[:, :], ALU.max).then_inc(mx_done, 1)
                    if ahead:
                        dve.wait_ge(q_done, G)
                    dve.reg_mov(t2, dve.snap(t1))
                    dve.reg_mov(b2, dve.snap(b1))
                    dve.reg_mov(t1, t)
                    dve.reg_mov(b1, b)
                    dve.reg_add(g, g, 1)
                dve.sem_inc(v_free[(s - 2) % RING], 1)

            with dve.Fori(0, TURNS) as k:
                for s in range(RING):
                    supertile(k, s, True)
            supertile(TURNS, 0, False)
            merge(dve.snap(g))
            rescale(dve.snap(g))
            dve.reg_mov(t2, dve.snap(t1))
            dve.reg_mov(b2, dve.snap(b1))
            dve.reg_add(g, g, 1)
            merge(dve.snap(g))
            dve.wait_ge(merged, dve.snap(g))

            step(nc.vector.tensor_scalar(rl[:, :], accv[:, 0:NB, 2 * F], TINY, None, ALU.max))
            nc.vector.reciprocal(rl[:, :], rl[:, :]).then_inc(all_merged, 1)

            dve.sem_inc(o_read, 2)

            def octet(o, par):
                w, w1, w2 = width(o), width(o - 1), width(o - 2)
                if w:
                    rows = y0[:, bass.ds(8 * o, w), :]
                    prodv = prod[:, 0:w * F].rearrange("p (b f) -> p b f", f=F)
                    dve.wait_ge(o_ready, o + 3)
                    nc.vector.tensor_tensor(rows, rows, psD[:, par, 0:w * F].rearrange("p (b f) -> p b f", f=F), ALU.add).then_inc(o_read, 1)
                if w1:
                    blk1 = bass.ds(8 * (o - 1), w1)
                    dve.wait_ge(sq_ready, o)
                    nc.vector.tensor_reduce(var[:, blk1], (sqd, um)[1 - par][:, 0:w1 * F].rearrange("p (b f) -> p b f", f=F), AX, ALU.add).then_inc(sq_summed, 1)
                if w:
                    dve.wait_ge(o_read, o + 3)
                    nc.vector.scalar_tensor_tensor(prodv, rows, 0.0, xt[:, bass.ds(8 * o, w), 1:ROW], ALU.max, ALU.add).then_inc(relu_done, 1)
                if w1:
                    dve.wait_ge(sq_summed, o)
                    nc.vector.tensor_scalar(var[:, blk1], var[:, blk1], 1.0 / F, EPS, ALU.mult, ALU.add).then_inc(var_done, 1)
                if w:
                    dve.wait_ge(relu_done, o + 1)
                    nc.vector.tensor_reduce(mean[:, 0:w], prodv, AX, ALU.add).then_inc(sum_done, 1)
                if w2:
                    blk2 = bass.ds(8 * (o - 2), w2)
                    dve.wait_ge(std_ready, o - 1)
                    nc.vector.reciprocal(rstd[:, blk2], rstd[:, blk2]).then_inc(rstd_done, 1)
                if w:
                    dve.wait_ge(sum_done, o + 1)
                    nc.vector.scalar_tensor_tensor(rows, mean[:, 0:w].unsqueeze(2).broadcast_to((P, w, F)), -1.0 / F, prodv, ALU.mult, ALU.add).then_inc(cen_done, 1)
                if w2:
                    dve.wait_ge(rstd_done, o - 1)
                    nc.vector.tensor_tensor(y0[:, blk2, :], y0[:, blk2, :], rstd[:, blk2].unsqueeze(2).broadcast_to((P, w2, F)), ALU.mult).then_inc(rows_ready, 1)

            octets(dve, octet, 2)

        @block.tensor
        def _(pe):
            pe.wait_ge(pool_step, 11)
            pe.wait_ge(w_in, 16 * 5)
            nc.tensor.transpose(psG[0:F, 0:P], wne[:, :], ident[:, :]).then_inc(wt_ready, 1)
            pe.wait_ge(wt_copied, 1)
            nc.tensor.matmul(psG[:, P:P + F], wneT[:, :], wo_z[:, :], start=True, stop=True).then_inc(wz_ready, 1)

            arrived = 0

            def x_arrives(upto):
                nonlocal arrived
                while arrived < len(chunks) and chunks[arrived][0] < upto:
                    b, n = chunks[arrived]
                    if n > 1 or b + n < NB:
                        pe.wait_ge(x_in[arrived], 16)
                    if b + n == NB:
                        pe.wait_ge(xr_in, 16)
                    arrived += 1

            def y_turn(n0, g, cnt, b):
                for par in range(cnt):
                    pe.wait_ge(xs_copied, n0 + par + 1)
                    for i in range(g):
                        last = nc.tensor.transpose(psT[0:F, par, i * P:(i + 1) * P], xt[:, b + 4 * par + i, 1:ROW], ident[:, :])
                    last.then_inc(xs_turned, 1)
                for par in range(cnt):
                    pe.wait_ge(xs_copied, n0 + par + 3)
                    pe.wait_ge(y_copied, n0 + par + 1)
                    for i in range(g):
                        last = nc.tensor.matmul(psD[:, par, i * F:(i + 1) * F], e1[0:F, par * 512 + i * P:par * 512 + (i + 1) * P],
                                                wo_x[:, :], start=True, stop=True)
                    last.then_inc(y_ready, 1)

            for o in range(OCT):
                x_arrives(8 * o + 8)
                y_turn(2 * o, 4, 2, 8 * o)
            x_arrives(NB)
            y_turn(2 * OCT, NR, 1, 8 * OCT)

            def stage_b(H, G, d):
                pe.wait_ge(pool_step, 11)
                pe.wait_ge(parts_done, H)
                if G is not None:
                    pe.wait_ge(u1_copied, G)
                nc.tensor.transpose(psTP, parts[:, :], identb[:, :]).then_inc(tp_done, 1)
                pe.wait_ge(tp_copied, H)
                for j in range(4):
                    last = nc.tensor.matmul(psU[:, j * P:(j + 1) * P], sel_u[:, j, :], partsT[:, :], start=True, stop=True)
                last.then_inc(bcu0, 1)
                for j in range(J):
                    last = nc.tensor.matmul(psD[:, d, j * P:(j + 1) * P], sel_d[:, j, :], partsT[:, :], start=True, stop=True)
                last.then_inc(bcd, 1)
                pe.wait_ge(u0_copied, H)
                for j in range(4):
                    last = nc.tensor.matmul(psU[:, j * P:(j + 1) * P], sel_u[:, 4 + j, :], partsT[:, :], start=True, stop=True)
                last.then_inc(bcu1, 1)

            g = pe.alloc_register("g_pe")
            h = pe.alloc_register("h_pe")
            coming = pe.alloc_register("coming_pe")
            count = pe.alloc_register("count_pe")
            slot = pe.alloc_register("slot_before")
            pe.reg_mov(slot, 0)
            pe.reg_mov(g, 1)
            pe.reg_mov(h, 2)
            pe.wait_ge(y_copied, 2 * OCT + 3)
            stage_b(1, None, 0)

            def multiply(G):
                sv = pe.snap(slot, min_val=0, max_val=RING - 1)
                pe.wait_ge(merged, G)
                for i in range(2):
                    pe.wait_ge(pt[i], G)
                    for j in range(4):
                        last = nc.tensor.matmul(psG[:, 0:AW], pT[:, i, j * P:(j + 1) * P],
                                                V[:, bass.ds(sv, 1), 4 * i + j, 1:VW].rearrange("p a f -> p (a f)"),
                                                start=(i == 0 and j == 0), stop=(i == 1 and j == 3))
                last.then_inc(agg_done, 1)

            def supertile(t, s, ahead):
                pe.reg_mov(count, pe.snap(coming))
                windows = pe.snap(count, min_val=1, max_val=NB)
                with pe.Fori(0, windows):
                    G, H = pe.snap(g), pe.snap(h)
                    if ahead:
                        stage_b(H, G, 1 - s % 2)
                    multiply(G)
                    pe.wait_ge(mx_done, G)
                    for i in range(2):
                        for j in range(4):
                            last = nc.tensor.transpose(psT[:, i, j * P:(j + 1) * P], e1[:, (4 * i + j) * P:(4 * i + j + 1) * P], ident[:, :])
                        last.then_inc(tr[i], 1)
                    if ahead:
                        pe.load(coming, trip[0:1, bass.ds(2 * t + 3, 1)])
                    pe.reg_mov(slot, s)
                    pe.reg_add(g, g, 1)
                    pe.reg_add(h, h, 1)

            pe.wait_ge(trip_in, 16)
            pe.load(coming, trip[0:1, 1:2])
            with pe.Fori(0, TURNS) as k:
                for s in range(RING):
                    supertile(RING * k + s, s, True)
            supertile(NT - 1, 0, False)

            multiply(pe.snap(g))

            pe.sem_inc(z_turned, 4)
            pe.sem_inc(o_ready, 2)

            def octet(o, par):
                w, w1 = width(o), width(o - 1)
                if w:
                    pe.wait_ge(z_ready, o + 1)
                for i in range(-(-w // 4)):
                    pe.wait_ge(z_copied, 2 * o + i + 1)
                    m = min(4, w - 4 * i)
                    for j in range(m):
                        last = nc.tensor.transpose(psT[:, i, j * P:(j + 1) * P], (e1, e2)[par][:, (4 * i + j) * P:(4 * i + j + 1) * P], ident[:, :])
                    last.then_inc(z_turned, 1)
                if w1:
                    pe.wait_ge(o_read, o)
                    for i in range(-(-w1 // 4)):
                        pe.wait_ge(z_copied, 2 * o + i + 1)
                        for j in range(4 * i, min(w1, 4 * i + 4)):
                            last = nc.tensor.matmul(psD[:, 1 - par, j * F:(j + 1) * F], ubc[:, 1 - par, j * P:(j + 1) * P],
                                                    wz[:, :], start=True, stop=True)
                    last.then_inc(o_ready, 1)

            octets(pe, octet, 1)


_INS = ['x', 'src', 'dst', 'edge_attr_64', 'L0_gnn_W_ne', 'L0_gnn_W_attn', 'L0_gnn_b_attn', 'L0_gnn_W_out']
_OUTS = [((12500, 64), 'float32')]


def kernel(**inputs):
    import numpy as _np
    import concourse.bacc as _bacc
    from concourse import mybir as _mybir
    from concourse.bass_utils import run_bass_kernel_spmd as _run

    nc = _bacc.Bacc("TRN2", target_bir_lowering=False, num_devices=1)
    arrays, args = {}, []
    for name in _INS:
        a = _np.ascontiguousarray(inputs[name])
        arrays[f"in_{name}_dram"] = a
        args.append(nc.dram_tensor(f"in_{name}_dram", a.shape, _mybir.dt.from_np(a.dtype), kind="ExternalInput").ap())
    for i, (shape, dtype) in enumerate(_OUTS):
        dt = _mybir.dt.from_np(_np.dtype(dtype))
        args.append(nc.dram_tensor(f"out_{i}_dram", shape, dt, kind="ExternalOutput").ap())
    graph_attention(nc, *args)
    r = _run(nc, [arrays], core_ids=[0])
    return r.results[0]["out_0_dram"]
```
